# Optimizing a Trainium2 kernel written in Bass

```python
import numpy as np
import jax
import jax.numpy as jnp

def _softmax(x, axis=-1):
    return jax.nn.softmax(x, axis=axis)

def _gelu(x):
    return jax.nn.gelu(x, approximate=True)

def _silu(x):
    return jax.nn.silu(x)

def _sigmoid(x):
    return jax.nn.sigmoid(x)

def _layernorm(x, axis=-1, eps=1e-05):
    m = jnp.mean(x, axis=axis, keepdims=True)
    v = jnp.var(x, axis=axis, keepdims=True)
    return (x - m) / jnp.sqrt(v + eps)

def _scatter_add(tgt, idx, src, axis=0):
    return tgt.at[idx].add(src)

def _segment_sum(src, seg, n):
    return jax.ops.segment_sum(src, seg, n)
kernel_name = 'mk_rec_standalone_d1_rec_r8_23d28b'

def setup_inputs(seed: int=0):
    np.random.seed(seed)
    _w = jnp.asarray

    def _rec_inputs():
        import jax
        import jax.numpy as jnp
        _rk = jax.random.key(seed)
        r_inputs = -0.000611745 + 1.00059 * jax.random.normal(jax.random.fold_in(_rk, 1), (2048, 39, 16), jnp.float32)
        return r_inputs
    r_inputs = _rec_inputs()

    def _L0_rec_setup():
        import jax, jax.numpy as jnp
        import numpy as np
        B, M, K = (512, 39, 16)
        CIN_LAYERS = [128, 128, 128]
        key = jax.random.key(seed)
        ks = jax.random.split(key, 8)
        inputs = jax.random.normal(ks[0], (B, M, K), jnp.float32)
        params = {}
        h = M
        for i, f in enumerate(CIN_LAYERS):
            params[f'W{i}'] = jax.random.normal(ks[1 + 2 * i], (h * M, f), jnp.float32) * 0.05
            params[f'b{i}'] = jnp.zeros((f,), jnp.float32)
            h = f // 2
        out_size = sum((f // 2 for f in CIN_LAYERS))
        params['W_lin'] = jax.random.normal(ks[7], (out_size, 1), jnp.float32) * 0.05
        return {'inputs': inputs, **params}
    _L0_rec_all = _L0_rec_setup()
    _L0_rec_in = {k: v for k, v in _L0_rec_all.items() if k in ('W0', 'b0', 'W1', 'b1', 'W2', 'b2', 'W_lin')}
    del _L0_rec_all
    return {'r_inputs': r_inputs, 'L0_rec_W0': _L0_rec_in['W0'], 'L0_rec_b0': _L0_rec_in['b0'], 'L0_rec_W1': _L0_rec_in['W1'], 'L0_rec_b1': _L0_rec_in['b1'], 'L0_rec_W2': _L0_rec_in['W2'], 'L0_rec_b2': _L0_rec_in['b2'], 'L0_rec_W_lin': _L0_rec_in['W_lin']}

def reference(r_inputs, L0_rec_W0, L0_rec_b0, L0_rec_W1, L0_rec_b1, L0_rec_W2, L0_rec_b2, L0_rec_W_lin):
    import jax
    import jax.numpy as jnp

    def _L0_rec_ref(inputs, W0, b0, W1, b1, W2, b2, W_lin):
        import jax, jax.numpy as jnp
        import numpy as np
        B, M, K = (512, 39, 16)
        CIN_LAYERS = [128, 128, 128]
        Ws = [W0, W1, W2]
        bs = [b0, b1, b2]
        x0 = inputs
        prev = inputs
        results = []
        for i, f in enumerate(CIN_LAYERS):
            h = prev.shape[1]
            Wr = Ws[i].reshape(h, M, f)
            z = jax.nn.relu(jnp.einsum('bhk,bmk,hmf->bfk', prev, x0, Wr) + bs[i][None, :, None])
            half = f // 2
            results.append(z[:, :half])
            prev = z[:, half:]
        pooled = jnp.sum(jnp.concatenate(results, axis=1), axis=-1)
        return pooled @ W_lin
    y = _L0_rec_ref(r_inputs, L0_rec_W0, L0_rec_b0, L0_rec_W1, L0_rec_b1, L0_rec_W2, L0_rec_b2, L0_rec_W_lin)
    return y

_drawn_inputs = setup_inputs


def setup_inputs(seed=0):
    import zlib

    import numpy as np

    out = dict(_drawn_inputs(seed))
    spreads = {'L0_rec_b0': (0.0, 0.1), 'L0_rec_b1': (0.0, 0.1), 'L0_rec_b2': (0.0, 0.458)}
    factors = {}
    for name, (base, spread) in spreads.items():
        noise = np.random.default_rng([zlib.crc32(name.encode()), seed]).standard_normal(out[name].shape)
        drawn = base * np.exp(spread * noise) if base else spread * noise
        out[name] = jnp.asarray(drawn.astype(out[name].dtype))
    for name, factor in factors.items():
        out[name] = (out[name] * factor).astype(out[name].dtype)
    return out
```

```python
from contextlib import ExitStack

import concourse.bass as bass
from concourse import mybir

F32 = mybir.dt.float32
ALU = mybir.AluOpType
ACT = mybir.ActivationFunctionType

P = 128
QUAD = 32
BANK = 512


def cin_kernel(nc, x, w0, w0_mirror, w1, w2, b0, b1, b2, w_lin, out, dims):
    BATCH, M, K, F = dims
    HALF = F // 2
    NBLK = x.shape[0]
    NB = x.shape[2]
    BB = NB // K
    D = (M + 1) // 2
    DPC = P // M
    C0 = -(-D // DPC)
    ROWS0 = [min(DPC, D - DPC * c) * M for c in range(C0)]
    QPT = P // QUAD
    T = -(-M // QPT)
    ROWS = [min(QPT, M - QPT * t) * QUAD for t in range(T)]
    CH = 2 * T
    NH = NB // BANK
    RING = 8
    U = 2
    assert NH == 2 and 2 * CH % RING == 0 and NBLK % U == 0 and HALF == 2 * QUAD and M % 2 == 1
    STEPS = NBLK // U
    PAIR_LOADS = 2 * DPC
    SMALL = 7
    TREE = (NB // BB).bit_length() - 2 + (BANK // BB).bit_length() - 2
    assert BATCH == P // QUAD * BANK

    with ExitStack() as ctx:
        def sb(name, shape):
            return ctx.enter_context(nc.sbuf_tensor(name, shape, F32))

        def ps(name, shape):
            return ctx.enter_context(nc.psum_tensor(name, shape, F32))

        def sem(name):
            return ctx.enter_context(nc.semaphore(name))

        w0_sb = sb("w0_sb", [P, C0, F])
        w0m_sb = sb("w0m_sb", [P, C0, F])
        w1_sb = sb("w1_sb", [P, CH, F])
        w2_sb = sb("w2_sb", [P, CH, HALF])
        bias = sb("bias", [P, 3])
        wl_col = sb("wl_col", [P, 2])
        ones = sb("ones", [P, QUAD])
        x_rep = sb("x_rep", [P, NB])
        x_rot = sb("x_rot", [P, C0, NB])
        x_bc = sb("x_bc", [P, U, T, NB])
        prev = [[sb(f"prev{l}{a}", [P, NB]) for a in range(2)] for l in (1, 2)]
        prod = sb("prod", [P, RING, NB])
        res01 = sb("res01", [P, NB])
        res2 = sb("res2", [P, BANK])
        sum01 = sb("sum01", [P, BB])
        sum2 = sb("sum2", [P, BB])
        pool01 = sb("pool01", [P, BATCH])
        pool2 = sb("pool2", [P, BATCH])
        y_sb = sb("y_sb", [P, BANK])

        acc0 = ps("acc0", [P, NH, BANK])
        acc1 = ps("acc1", [P, NH, BANK])
        acc2 = ps("acc2", [P, BANK])
        acc_y = ps("acc_y", [P, BANK])

        w0_loaded = sem("w0_loaded")
        w0_cleared = sem("w0_cleared")
        w0_ready = sem("w0_ready")
        w1_loaded = sem("w1_loaded")
        w2_loaded = sem("w2_loaded")
        small_loaded = sem("small_loaded")
        ones_ready = sem("ones_ready")
        pairs_loaded = sem("pairs_loaded")
        bc_loaded = [sem(f"bc_loaded{u}") for u in range(U)]
        prod0_ready = sem("prod0_ready")
        prod_ready = sem("prod_ready")
        chunk_used = sem("chunk_used")
        acc0_full = sem("acc0_full")
        prev_ready = [sem(f"prev{l}_ready") for l in (1, 2)]
        res01_ready = sem("res01_ready")
        res2_ready = sem("res2_ready")
        tree = sem("tree")
        sum01_ready = sem("sum01_ready")
        sum2_ready = sem("sum2_ready")
        pooled = sem("pooled")
        y_ready = sem("y_ready")
        y_copied = sem("y_copied")
        y_stored = sem("y_stored")

        block = ctx.enter_context(nc.Block())

        @block.sync
        def _(sp):
            def load_pairs(i):
                for d in range(DPC):
                    rows = slice(M * d, M * d + M)
                    nc_d = (D - 1 - d) // DPC + 1
                    base = x[i, d:d + 1, :]
                    sp.dma_start(x_rep[rows, :], x[i, 0:M, :]).then_inc(pairs_loaded, 16)
                    src = bass.AP(tensor=base.tensor, offset=base.offset, ap=[[NB, M], [DPC * NB, nc_d], [1, NB]])
                    sp.dma_start(x_rot[rows, 0:nc_d, :], src).then_inc(pairs_loaded, 16)

            def load_bc(i, u):
                for q in range(QPT):
                    nt = (M - 1 - q) // QPT + 1
                    base = x[i, q:q + 1, :]
                    src = bass.AP(tensor=base.tensor, offset=base.offset, ap=[[0, QUAD], [QPT * NB, nt], [1, NB]])
                    sp.dma_start(x_bc[QUAD * q:QUAD * q + QUAD, u, 0:nt, :], src).then_inc(bc_loaded[u], 16)

            for c in range(C0):
                r = ROWS0[c]
                sp.dma_start(w0_sb[0:r, c, :], w0[DPC * M * c:DPC * M * c + r, :]).then_inc(w0_loaded, 16)
                lo = M if c == 0 else 0
                sp.dma_start(w0m_sb[lo:r, c, :],
                             w0_mirror[DPC * M * c + lo:DPC * M * c + r, :]).then_inc(w0_loaded, 16)
            load_pairs(0)
            sp.dma_start(bias[:, 0:1], b0).then_inc(small_loaded, 16)
            sp.dma_start(bias[:, 1:2], b1).then_inc(small_loaded, 16)
            for g in range(2):
                sp.dma_start(bias[HALF * g:HALF * g + HALF, 2:3], b2[0:HALF, :]).then_inc(small_loaded, 16)
                sp.dma_start(wl_col[HALF * g:HALF * g + HALF, 1:2],
                             w_lin[2 * HALF:3 * HALF, :]).then_inc(small_loaded, 16)
            sp.dma_start(wl_col[:, 0:1], w_lin[0:2 * HALF, :]).then_inc(small_loaded, 16)
            load_bc(0, 0)
            sp.dma_start(w1_sb[:], w1).then_inc(w1_loaded, 16)
            sp.wait_ge(acc0_full, 1)
            load_pairs(1)
            load_bc(1, 1)
            sp.dma_start(w2_sb[:], w2).then_inc(w2_loaded, 16)

            with sp.Fori(0, STEPS - 1) as j:
                for u in range(U):
                    i = j * U + u
                    sp.wait_ge(acc0_full, i + 2)
                    load_pairs(i + 2)
                    sp.wait_ge(prod_ready, i * (2 * CH) + 2 * CH)
                    load_bc(i + 2, u)

            sp.wait_ge(y_copied, 1)
            y_rows = y_sb[0:P - QUAD + 1:QUAD, :]
            sp.dma_start(out, y_rows).then_inc(y_stored, 16)
            sp.wait_ge(y_stored, 16)

        @block.vector
        def _(dve):
            def products0(i):
                dve.wait_ge(pairs_loaded, i * (16 * PAIR_LOADS) + 16 * PAIR_LOADS)
                for c in range(C0):
                    r = x_rot[0:ROWS0[c], c, :]
                    nc.vector.tensor_tensor(r, r, x_rep[0:ROWS0[c], :], ALU.mult).then_inc(prod0_ready, 1)

            def products(i, j, u, layer):
                if layer == 1:
                    dve.wait_ge(bc_loaded[u], j * (16 * QPT) + 16 * QPT)
                first = i * (2 * CH) + (layer - 1) * CH
                for c in range(CH):
                    a, t = divmod(c, T)
                    if t == 0:
                        dve.wait_ge(prev_ready[layer - 1], i * 2 + a + 1)
                    dve.wait_ge(chunk_used, first + c + 1)
                    k = ROWS[t]
                    nc.vector.tensor_tensor(prod[0:k, ((layer - 1) * CH + c) % RING, :], prev[layer - 1][a][0:k, :],
                                            x_bc[0:k, u, t, :], ALU.mult).then_inc(prod_ready, 1)

            nc.vector.memset(ones[:], 1.0).then_inc(ones_ready, 1)
            nc.vector.memset(w0m_sb[0:M, 0, :], 0.0).then_inc(w0_cleared, 1)
            dve.wait_ge(w0_cleared, 1)
            dve.wait_ge(w0_loaded, 2 * 16 * C0)
            for c in range(C0):
                r = ROWS0[c]
                nc.vector.tensor_tensor(w0_sb[0:r, c, :], w0_sb[0:r, c, :], w0m_sb[0:r, c, :],
                                        ALU.add).then_inc(w0_ready, 1)
            products0(0)
            with dve.Fori(0, STEPS - 1) as j:
                for u in range(U):
                    i = j * U + u
                    products(i, j, u, 1)
                    products0(i + 1)
                    products(i, j, u, 2)
            for u in range(U):
                i = (STEPS - 1) * U + u
                products(i, STEPS - 1, u, 1)
                if u < U - 1:
                    products0(i + 1)
                products(i, STEPS - 1, u, 2)

            dve.wait_ge(y_ready, 1)
            nc.vector.tensor_copy(y_sb[:], acc_y[:]).then_inc(y_copied, 1)

        @block.tensor
        def _(pe):
            def layer0(i, first=False):
                if not first:
                    pe.wait_ge(res01_ready, i * 2)
                for c in range(C0):
                    pe.wait_ge(prod0_ready, i * C0 + c + 1)
                    k = ROWS0[c]
                    for h in range(NH):
                        mm = nc.tensor.matmul(acc0[:, h, :], w0_sb[0:k, c, :],
                                              x_rot[0:k, c, BANK * h:BANK * h + BANK],
                                              start=(c == 0), stop=(c == C0 - 1))
                mm.then_inc(acc0_full, 1)

            def layer1(i):
                pe.wait_ge(res01_ready, i * 2 + 1)
                for c in range(CH):
                    pe.wait_ge(prod_ready, i * (2 * CH) + c + 1)
                    k = ROWS[c % T]
                    for h in range(NH):
                        mm = nc.tensor.matmul(acc1[:, h, :], w1_sb[0:k, c, :],
                                              prod[0:k, c % RING, BANK * h:BANK * h + BANK],
                                              start=(c == 0), stop=(c == CH - 1))
                    mm.then_inc(chunk_used, 1)

            def layer2(i):
                pe.wait_ge(res2_ready, i + 1)
                for c in range(CH):
                    pe.wait_ge(prod_ready, i * (2 * CH) + CH + c + 1)
                    k = ROWS[c % T]
                    for h in range(NH):
                        mm = nc.tensor.matmul(acc2[HALF * h:HALF * h + HALF, :], w2_sb[0:k, c, :],
                                              prod[0:k, (CH + c) % RING, BANK * h:BANK * h + BANK],
                                              start=(c == 0), stop=(c == CH - 1))
                    mm.then_inc(chunk_used, 1)

            pe.sem_inc(chunk_used, RING)
            pe.wait_ge(w0_ready, C0)
            layer0(0, first=True)
            pe.wait_ge(w1_loaded, 16)
            pe.wait_ge(w2_loaded, 16)
            with pe.Fori(0, STEPS - 1) as j:
                for u in range(U):
                    i = j * U + u
                    layer1(i)
                    layer0(i + 1)
                    layer2(i)
            for u in range(U):
                i = (STEPS - 1) * U + u
                layer1(i)
                if u < U - 1:
                    layer0(i + 1)
                layer2(i)

            pe.wait_ge(ones_ready, 1)
            pe.wait_ge(pooled, 2 * NBLK)
            for g, pool in enumerate((pool01, pool2)):
                for q in range(P // QUAD):
                    mm = nc.tensor.matmul(acc_y[QUAD * q:QUAD * q + QUAD, :], ones[:],
                                          pool[:, BANK * q:BANK * q + BANK],
                                          start=(g == 0), stop=(g == 1))
            mm.then_inc(y_ready, 1)

        @block.scalar
        def _(act):
            def spread(dst, acc, layer):
                src = acc[HALF:P, :, :].rearrange("p h n -> p (h n)")
                for g in range(2):
                    op = nc.scalar.activation(dst[0][HALF * g:HALF * g + HALF, :], src, ACT.Relu,
                                              bias=bias[HALF:P, layer:layer + 1])
                op.then_inc(prev_ready[layer], 1)
                for q in range(QPT):
                    h = HALF + QUAD * ((q + 1) % 2)
                    op = nc.scalar.activation(dst[1][QUAD * q:QUAD * q + QUAD, :],
                                              acc[h:h + QUAD, :, :].rearrange("p h n -> p (h n)"), ACT.Relu,
                                              bias=bias[h:h + QUAD, layer:layer + 1])
                op.then_inc(prev_ready[layer], 1)

            def keep01(acc, layer):
                nc.scalar.activation(res01[HALF * layer:HALF * layer + HALF, :],
                                     acc[0:HALF, :, :].rearrange("p h n -> p (h n)"), ACT.Relu,
                                     bias=bias[0:HALF, layer:layer + 1]).then_inc(res01_ready, 1)

            def evacuate0(i):
                act.wait_ge(acc0_full, i + 1)
                spread(prev[0], acc0, 0)
                act.wait_ge(sum01_ready, i + 1)
                keep01(acc0, 0)

            def evacuate1(i):
                act.wait_ge(chunk_used, i * (2 * CH) + RING + CH)
                spread(prev[1], acc1, 1)
                keep01(acc1, 1)

            def evacuate2(i):
                act.wait_ge(chunk_used, i * (2 * CH) + RING + 2 * CH)
                act.wait_ge(sum2_ready, i + 1)
                nc.scalar.activation(res2[:], acc2[:], ACT.Relu, bias=bias[:, 2:3]).then_inc(res2_ready, 1)

            def weigh(i, pool, total, ready, g):
                act.wait_ge(ready, i + 2)
                act.wait_ge(small_loaded, 16 * SMALL)
                nc.scalar.activation(pool[:, bass.ds(i * BB, BB)], total[:], ACT.Copy,
                                     scale=wl_col[:, g:g + 1]).then_inc(pooled, 1)

            act.sem_inc(res01_ready, 1)
            act.sem_inc(res2_ready, 1)
            act.wait_ge(small_loaded, 16 * SMALL)
            evacuate0(0)
            with act.Fori(0, STEPS - 1) as j:
                for u in range(U):
                    i = j * U + u
                    evacuate1(i)
                    evacuate0(i + 1)
                    weigh(i, pool01, sum01, sum01_ready, 0)
                    evacuate2(i)
                    weigh(i, pool2, sum2, sum2_ready, 1)
            for u in range(U):
                i = (STEPS - 1) * U + u
                evacuate1(i)
                if u < U - 1:
                    evacuate0(i + 1)
                weigh(i, pool01, sum01, sum01_ready, 0)
                evacuate2(i)
                weigh(i, pool2, sum2, sum2_ready, 1)

        @block.gpsimd
        def _(pool):
            def channel_sum(buf, total, width, step, done):
                n = 0
                while width > 2 * BB:
                    width //= 2
                    nc.gpsimd.tensor_tensor(buf[:, 0:width], buf[:, 0:width], buf[:, width:2 * width],
                                            ALU.add).then_inc(tree, 1)
                    n += 1
                    pool.wait_ge(tree, step + n)
                nc.gpsimd.tensor_tensor(total[:], buf[:, 0:BB], buf[:, BB:2 * BB], ALU.add).then_inc(done, 1)
                return n

            pool.sem_inc(sum01_ready, 1)
            pool.sem_inc(sum2_ready, 1)
            with pool.Fori(0, NBLK) as i:
                pool.wait_ge(res01_ready, i * 2 + 3)
                n = channel_sum(res01, sum01, NB, i * TREE, sum01_ready)
                pool.wait_ge(res2_ready, i + 2)
                channel_sum(res2, sum2, BANK, i * TREE + n, sum2_ready)


def kernel(r_inputs, L0_rec_W0, L0_rec_b0, L0_rec_W1, L0_rec_b1, L0_rec_W2, L0_rec_b2, L0_rec_W_lin):
    import numpy as np
    import concourse.bacc as bacc
    from concourse.bass_utils import run_bass_kernel_spmd

    x, W0, W1, W2 = (np.asarray(a) for a in (r_inputs, L0_rec_W0, L0_rec_W1, L0_rec_W2))
    BATCH, M, K = x.shape
    F = W0.shape[1]
    H = F // 2
    BB = 1024 // K

    D = (M + 1) // 2
    xb = x.reshape(BATCH // BB, BB, M, K).transpose(0, 2, 3, 1).reshape(BATCH // BB, M, K * BB)
    xb = np.concatenate([xb, xb[:, 0:D - 1]], axis=1)

    d, i = np.divmod(np.arange(D * M), M)
    W0 = W0.reshape(M, M, F)
    w0, w0_mirror = W0[i, (i + d) % M], W0[(i + d) % M, i]

    T = -(-M // 4)
    a, t, q, r = np.meshgrid(np.arange(2), np.arange(T), np.arange(4), np.arange(32), indexing="ij")
    row = ((32 * ((q + a) % 2) + r) * M + np.minimum(4 * t + q, M - 1)).reshape(2 * T, 128)
    w1, w2 = W1[row].transpose(1, 0, 2), W2[row][:, :, 0:H].transpose(1, 0, 2)

    ins = {"x": xb, "w0": w0, "w0_mirror": w0_mirror, "w1": w1, "w2": w2,
           "b0": np.asarray(L0_rec_b0).reshape(F, 1), "b1": np.asarray(L0_rec_b1).reshape(F, 1),
           "b2": np.asarray(L0_rec_b2).reshape(F, 1), "w_lin": np.asarray(L0_rec_W_lin)}
    nc = bacc.Bacc("TRN2", target_bir_lowering=False, num_devices=1)
    arrays, args = {}, []
    for name, v in ins.items():
        arrays[name] = np.ascontiguousarray(v)
        args.append(nc.dram_tensor(name, v.shape, mybir.dt.from_np(v.dtype), kind="ExternalInput").ap())
    args.append(nc.dram_tensor("out", (4, BATCH // 4), F32, kind="ExternalOutput").ap())
    cin_kernel(nc, *args, (BATCH, M, K, F))
    r = run_bass_kernel_spmd(nc, [arrays], core_ids=[0])
    return r.results[0]["out"].reshape(BATCH, 1)
```

```python
from contextlib import ExitStack

import concourse.bass as bass
from concourse import mybir

F32 = mybir.dt.float32
ALU = mybir.AluOpType
ACT = mybir.ActivationFunctionType

P = 128
QUAD = 32
BANK = 512


def cin_kernel(nc, x, w0, w0_mirror, w1, w2, b0, b1, b2, w_lin, out, dims):
    BATCH, M, K, F = dims
    HALF = F // 2
    NBLK = x.shape[0]
    NB = x.shape[2]
    BB = NB // K
    D = (M + 1) // 2
    DPC = P // M
    C0 = (D - 2) // DPC
    IC = M - QUAD
    ROWS0 = [DPC * M + (IC if c < 2 else 0) for c in range(C0)]
    QPT = P // QUAD
    T = M // QPT
    T2, T1 = T, T + 1
    CHUNKS = [(0, t) for t in range(T)] + [(0, T2)] + [(1, t) for t in range(T)] + [(0, T1)]
    CH = len(CHUNKS)
    X0_GROUPS = [(0, 1), (1, 2), (2, C0)]
    XB_GROUPS = [(0, 1), (1, 3), (3, 5), (5, T)]
    NH = NB // BANK
    RING = 8
    U = 2
    assert NH == 2 and 2 * CH % RING == 0 and NBLK % U == 0 and HALF == 2 * QUAD and M == QPT * T + 3
    assert D == DPC * C0 + 2 and DPC * M + IC <= P
    STEPS = NBLK // U
    ROT_LOADS = [DPC + 1, DPC + 1, DPC]
    BC_LOADS = [QPT] * len(XB_GROUPS) + [3]
    SMALL = 7
    TREE = (NB // BB).bit_length() - 2 + (BANK // BB).bit_length() - 2
    assert BATCH == P // QUAD * BANK

    with ExitStack() as ctx:
        def sb(name, shape):
            return ctx.enter_context(nc.sbuf_tensor(name, shape, F32))

        def ps(name, shape):
            return ctx.enter_context(nc.psum_tensor(name, shape, F32))

        def sem(name):
            return ctx.enter_context(nc.semaphore(name))

        w0_sb = sb("w0_sb", [P, C0 + 1, F])
        w0m_sb = sb("w0m_sb", [P, C0 + 1, F])
        w1_sb = sb("w1_sb", [P, CH, F])
        w2_sb = sb("w2_sb", [P, CH, HALF])
        bias = sb("bias", [P, 3])
        wl_col = sb("wl_col", [P, 2])
        ones = sb("ones", [P, QUAD])
        x_rep = sb("x_rep", [P, NB])
        x_rot = sb("x_rot", [P, C0, NB])
        x_rep_s = sb("x_rep_s", [P, BANK])
        x_rot_s = sb("x_rot_s", [P, BANK])
        x_bc = sb("x_bc", [P, U, T + 2, NB])
        prev = [[sb(f"prev{l}{a}", [P, NB]) for a in range(2)] for l in (1, 2)]
        prod = sb("prod", [P, RING, NB])
        res01 = sb("res01", [P, NB])
        res2 = sb("res2", [P, BANK])
        sum01 = sb("sum01", [P, BB])
        sum2 = sb("sum2", [P, BB])
        pool01 = sb("pool01", [P, BATCH])
        pool2 = sb("pool2", [P, BATCH])
        y_sb = sb("y_sb", [P, BANK])

        acc0 = ps("acc0", [P, NH, BANK])
        acc1 = ps("acc1", [P, NH, BANK])
        acc2 = ps("acc2", [P, BANK])
        acc_y = ps("acc_y", [P, BANK])

        w0_loaded = sem("w0_loaded")
        w0_cleared = sem("w0_cleared")
        w0_ready = sem("w0_ready")
        w1_loaded = sem("w1_loaded")
        w2_loaded = sem("w2_loaded")
        small_loaded = sem("small_loaded")
        ones_ready = sem("ones_ready")
        split_loaded = sem("split_loaded")
        rep_loaded = sem("rep_loaded")
        rot_loaded = [sem(f"rot_loaded{g}") for g in range(len(X0_GROUPS))]
        bc_loaded = [[sem(f"bc_loaded{u}{g}") for g in range(len(XB_GROUPS) + 1)]
                     for u in range(U)]
        prod0_ready = sem("prod0_ready")
        prod_ready = sem("prod_ready")
        chunk_used = sem("chunk_used")
        acc0_full = sem("acc0_full")
        prev_ready = [sem(f"prev{l}_ready") for l in (1, 2)]
        res01_ready = sem("res01_ready")
        res2_ready = sem("res2_ready")
        tree = sem("tree")
        sum01_ready = sem("sum01_ready")
        sum2_ready = sem("sum2_ready")
        pooled = sem("pooled")
        y_ready = sem("y_ready")
        y_copied = sem("y_copied")
        y_stored = sem("y_stored")

        block = ctx.enter_context(nc.Block())

        @block.sync
        def _(sp):
            def rows_of(i, first, ap, col=0):
                base = x[i, first:first + 1, col:NB]
                return bass.AP(tensor=base.tensor, offset=base.offset, ap=ap)

            def load_pairs(i):
                for h in range(NH):
                    rows = slice(HALF * h, HALF * h + HALF)
                    src = rows_of(i, IC, [[NB, QUAD], [0, 2], [1, BANK]], BANK * h)
                    sp.dma_start(x_rep_s[rows, :], src).then_inc(split_loaded, 16)
                    src = rows_of(i, IC + D - 2, [[NB, QUAD], [NB, 2], [1, BANK]], BANK * h)
                    sp.dma_start(x_rot_s[rows, :], src).then_inc(split_loaded, 16)
                for r, n in ((0, 48), (48, 48), (96, ROWS0[0] - 96)):
                    sp.dma_start(x_rep[r:r + n, :], x[i, r % M:r % M + n, :]).then_inc(rep_loaded, 16)
                for g, (c0, c1) in enumerate(X0_GROUPS):
                    for d in range(DPC):
                        src = rows_of(i, DPC * c0 + d, [[NB, M], [DPC * NB, c1 - c0], [1, NB]])
                        sp.dma_start(x_rot[M * d:M * d + M, c0:c1, :], src).then_inc(rot_loaded[g], 16)
                    if g < 2:
                        src = x[i, D - 2 + g:D - 2 + g + IC, :]
                        sp.dma_start(x_rot[DPC * M:DPC * M + IC, g, :], src).then_inc(rot_loaded[g], 16)

            def load_bc(i, u):
                for g, (t0, t1) in enumerate(XB_GROUPS):
                    for q in range(QPT):
                        src = rows_of(i, QPT * t0 + q, [[0, QUAD], [QPT * NB, t1 - t0], [1, NB]])
                        sp.dma_start(x_bc[QUAD * q:QUAD * q + QUAD, u, t0:t1, :], src).then_inc(bc_loaded[u][g], 16)
                for q in range(2):
                    src = rows_of(i, QPT * T + q, [[0, HALF], [1, NB]])
                    sp.dma_start(x_bc[HALF * q:HALF * q + HALF, u, T2, :], src).then_inc(bc_loaded[u][-1], 16)
                src = rows_of(i, M - 1, [[0, P], [1, NB]])
                sp.dma_start(x_bc[:, u, T1, :], src).then_inc(bc_loaded[u][-1], 16)

            load_pairs(0)
            sp.dma_start(w1_sb[:], w1).then_inc(w1_loaded, 16)
            load_bc(0, 0)
            sp.dma_start(w2_sb[:], w2).then_inc(w2_loaded, 16)
            sp.wait_ge(acc0_full, 1)
            load_pairs(1)
            load_bc(1, 1)
            with sp.Fori(0, STEPS - 1) as j:
                for u in range(U):
                    i = j * U + u
                    sp.wait_ge(acc0_full, i + 2)
                    load_pairs(i + 2)
                    sp.wait_ge(prod_ready, i * (2 * CH) + 2 * CH)
                    load_bc(i + 2, u)

            sp.wait_ge(y_copied, 1)
            y_rows = y_sb[0:P - QUAD + 1:QUAD, :]
            sp.dma_start(out, y_rows).then_inc(y_stored, 16)
            sp.wait_ge(y_stored, 16)

        @block.vector
        def _(dve):
            def products0(i):
                dve.wait_ge(split_loaded, i * (32 * NH) + 32 * NH)
                nc.vector.tensor_tensor(x_rot_s[:], x_rot_s[:], x_rep_s[:], ALU.mult).then_inc(prod0_ready, 1)
                dve.wait_ge(rep_loaded, i * (16 * 3) + 16 * 3)
                for g, (c0, c1) in enumerate(X0_GROUPS):
                    dve.wait_ge(rot_loaded[g], i * (16 * ROT_LOADS[g]) + 16 * ROT_LOADS[g])
                    for c in range(c0, c1):
                        r = x_rot[0:ROWS0[c], c, :]
                        nc.vector.tensor_tensor(r, r, x_rep[0:ROWS0[c], :], ALU.mult).then_inc(prod0_ready, 1)

            def products(i, j, u, layer):
                first = i * (2 * CH) + (layer - 1) * CH
                group = {t0: g for g, (t0, _) in enumerate(XB_GROUPS)}
                group[T2] = len(XB_GROUPS)
                for c, (a, t) in enumerate(CHUNKS):
                    if layer == 1 and a == 0 and t in group:
                        n = 16 * BC_LOADS[group[t]]
                        dve.wait_ge(bc_loaded[u][group[t]], j * n + n)
                    if t == 0:
                        dve.wait_ge(prev_ready[layer - 1], i * 2 + a + 1)
                    dve.wait_ge(chunk_used, first + c + 1)
                    s = ((layer - 1) * CH + c) % RING
                    old, new = prev[layer - 1][a], x_bc[:, u, t, :]
                    if t < T1:
                        mul = nc.vector.tensor_tensor(prod[:, s, :], old[:], new, ALU.mult)
                    elif layer == 2:
                        mul = nc.vector.tensor_tensor(prod[0:HALF, s, :], old[0:HALF, :], new[0:HALF], ALU.mult)
                    else:
                        for h in range(NH):
                            k, n = slice(HALF * h, HALF * h + HALF), slice(BANK * h, BANK * h + BANK)
                            mul = nc.vector.tensor_tensor(prod[k, s, n], old[k, n], new[k, n], ALU.mult)
                    mul.then_inc(prod_ready, 1)

            nc.vector.memset(ones[:], 1.0).then_inc(ones_ready, 1)
            dve.wait_ge(w0_loaded, 32)
            nc.vector.memset(w0m_sb[0:M, 0, :], 0.0).then_inc(w0_cleared, 1)
            dve.wait_ge(w0_cleared, 1)
            nc.vector.tensor_tensor(w0_sb[:], w0_sb[:], w0m_sb[:], ALU.add).then_inc(w0_ready, 1)
            products0(0)
            with dve.Fori(0, STEPS - 1) as j:
                for u in range(U):
                    i = j * U + u
                    products(i, j, u, 1)
                    products0(i + 1)
                    products(i, j, u, 2)
            for u in range(U):
                i = (STEPS - 1) * U + u
                products(i, STEPS - 1, u, 1)
                if u < U - 1:
                    products0(i + 1)
                products(i, STEPS - 1, u, 2)

            dve.wait_ge(y_ready, 1)
            nc.vector.tensor_copy(y_sb[:], acc_y[:]).then_inc(y_copied, 1)

        @block.tensor
        def _(pe):
            def split(acc, w, rhs, start, stop):
                for h in range(NH):
                    k = slice(HALF * h, HALF * h + HALF)
                    mm = nc.tensor.matmul(acc[:, h, :], w[k, :], rhs[h], start=start, stop=stop)
                return mm

            def full(acc, w, rhs, start, stop):
                for h in range(NH):
                    mm = nc.tensor.matmul(acc[:, h, :], w, rhs[:, BANK * h:BANK * h + BANK], start=start, stop=stop)
                return mm

            def layer0(i, first=False):
                if not first:
                    pe.wait_ge(res01_ready, i * 2)
                pe.wait_ge(prod0_ready, i * (C0 + 1) + 1)
                split(acc0, w0_sb[:, C0, :], [x_rot_s[0:HALF, :], x_rot_s[HALF:P, :]], True, False)
                for c in range(C0):
                    pe.wait_ge(prod0_ready, i * (C0 + 1) + c + 2)
                    k = ROWS0[c]
                    mm = full(acc0, w0_sb[0:k, c, :], x_rot[0:k, c, :], False, c == C0 - 1)
                mm.then_inc(acc0_full, 1)

            def layer1(i):
                pe.wait_ge(res01_ready, i * 2 + 1)
                for c in range(CH):
                    pe.wait_ge(prod_ready, i * (2 * CH) + c + 1)
                    s = c % RING
                    if c < CH - 1:
                        mm = full(acc1, w1_sb[:, c, :], prod[:, s, :], c == 0, False)
                    else:
                        mm = split(acc1, w1_sb[:, c, :], [prod[0:HALF, s, 0:BANK], prod[HALF:P, s, BANK:NB]],
                                   False, True)
                    mm.then_inc(chunk_used, 1)

            def layer2(i):
                pe.wait_ge(w2_loaded, 16)
                pe.wait_ge(res2_ready, i + 1)
                for c in range(CH):
                    if c < CH - 1:
                        pe.wait_ge(prod_ready, i * (2 * CH) + CH + (c + 1 if c < CH - 2 else CH))
                    k = P if c < CH - 1 else HALF
                    for h in range(NH):
                        mm = nc.tensor.matmul(acc2[HALF * h:HALF * h + HALF, :], w2_sb[0:k, c, :],
                                              prod[0:k, (CH + c) % RING, BANK * h:BANK * h + BANK],
                                              start=(c == 0), stop=(c == CH - 1))
                    mm.then_inc(chunk_used, 1)

            pe.sem_inc(chunk_used, RING)
            pe.wait_ge(w0_ready, 1)
            layer0(0, first=True)
            pe.wait_ge(w1_loaded, 16)
            with pe.Fori(0, STEPS - 1) as j:
                for u in range(U):
                    i = j * U + u
                    layer1(i)
                    layer0(i + 1)
                    layer2(i)
            for u in range(U):
                i = (STEPS - 1) * U + u
                layer1(i)
                if u < U - 1:
                    layer0(i + 1)
                layer2(i)

            pe.wait_ge(ones_ready, 1)
            for g, pool in enumerate((pool01, pool2)):
                pe.wait_ge(pooled, 2 * NBLK - 1 + g)
                for q in range(P // QUAD):
                    mm = nc.tensor.matmul(acc_y[QUAD * q:QUAD * q + QUAD, :], ones[:],
                                          pool[:, BANK * q:BANK * q + BANK],
                                          start=(g == 0), stop=(g == 1))
            mm.then_inc(y_ready, 1)

        @block.scalar
        def _(act):
            def spread(dst, acc, layer):
                src = acc[HALF:P, :, :].rearrange("p h n -> p (h n)")
                for g in range(2):
                    op = nc.scalar.activation(dst[0][HALF * g:HALF * g + HALF, :], src, ACT.Relu,
                                              bias=bias[HALF:P, layer:layer + 1])
                op.then_inc(prev_ready[layer], 1)
                for q in range(QPT):
                    h = HALF + QUAD * ((q + 1) % 2)
                    op = nc.scalar.activation(dst[1][QUAD * q:QUAD * q + QUAD, :],
                                              acc[h:h + QUAD, :, :].rearrange("p h n -> p (h n)"), ACT.Relu,
                                              bias=bias[h:h + QUAD, layer:layer + 1])
                op.then_inc(prev_ready[layer], 1)

            def keep01(acc, layer):
                nc.scalar.activation(res01[HALF * layer:HALF * layer + HALF, :],
                                     acc[0:HALF, :, :].rearrange("p h n -> p (h n)"), ACT.Relu,
                                     bias=bias[0:HALF, layer:layer + 1]).then_inc(res01_ready, 1)

            def evacuate0(i):
                act.wait_ge(acc0_full, i + 1)
                spread(prev[0], acc0, 0)
                act.wait_ge(sum01_ready, i + 1)
                keep01(acc0, 0)

            def evacuate1(i):
                act.wait_ge(chunk_used, i * (2 * CH) + RING + CH)
                spread(prev[1], acc1, 1)
                keep01(acc1, 1)

            def evacuate2(i):
                act.wait_ge(chunk_used, i * (2 * CH) + RING + 2 * CH)
                act.wait_ge(sum2_ready, i + 1)
                nc.scalar.activation(res2[:], acc2[:], ACT.Relu, bias=bias[:, 2:3]).then_inc(res2_ready, 1)

            def weigh(i, pool, total, ready, g):
                act.wait_ge(ready, i + 2)
                act.wait_ge(small_loaded, 16 * SMALL)
                nc.scalar.activation(pool[:, bass.ds(i * BB, BB)], total[:], ACT.Copy,
                                     scale=wl_col[:, g:g + 1]).then_inc(pooled, 1)

            act.dma_start(w0_sb[:], w0).then_inc(w0_loaded, 16)
            act.dma_start(w0m_sb[:], w0_mirror).then_inc(w0_loaded, 16)
            act.dma_start(bias[:, 0:1], b0).then_inc(small_loaded, 16)
            act.dma_start(bias[:, 1:2], b1).then_inc(small_loaded, 16)
            for g in range(2):
                act.dma_start(bias[HALF * g:HALF * g + HALF, 2:3], b2[0:HALF, :]).then_inc(small_loaded, 16)
                act.dma_start(wl_col[HALF * g:HALF * g + HALF, 1:2],
                              w_lin[2 * HALF:3 * HALF, :]).then_inc(small_loaded, 16)
            act.dma_start(wl_col[:, 0:1], w_lin[0:2 * HALF, :]).then_inc(small_loaded, 16)
            act.sem_inc(res01_ready, 1)
            act.sem_inc(res2_ready, 1)
            act.wait_ge(small_loaded, 16 * SMALL)
            evacuate0(0)
            with act.Fori(0, STEPS - 1) as j:
                for u in range(U):
                    i = j * U + u
                    evacuate1(i)
                    evacuate0(i + 1)
                    weigh(i, pool01, sum01, sum01_ready, 0)
                    evacuate2(i)
                    weigh(i, pool2, sum2, sum2_ready, 1)
            for u in range(U):
                i = (STEPS - 1) * U + u
                evacuate1(i)
                if u < U - 1:
                    evacuate0(i + 1)
                weigh(i, pool01, sum01, sum01_ready, 0)
                evacuate2(i)
                weigh(i, pool2, sum2, sum2_ready, 1)

        @block.gpsimd
        def _(pool):
            def channel_sum(buf, total, width, step, done):
                n = 0
                while width > 2 * BB:
                    width //= 2
                    nc.gpsimd.tensor_tensor(buf[:, 0:width], buf[:, 0:width], buf[:, width:2 * width],
                                            ALU.add).then_inc(tree, 1)
                    n += 1
                    pool.wait_ge(tree, step + n)
                nc.gpsimd.tensor_tensor(total[:], buf[:, 0:BB], buf[:, BB:2 * BB], ALU.add).then_inc(done, 1)
                return n

            pool.sem_inc(sum01_ready, 1)
            pool.sem_inc(sum2_ready, 1)
            with pool.Fori(0, NBLK) as i:
                pool.wait_ge(res01_ready, i * 2 + 3)
                n = channel_sum(res01, sum01, NB, i * TREE, sum01_ready)
                pool.wait_ge(res2_ready, i + 2)
                channel_sum(res2, sum2, BANK, i * TREE + n, sum2_ready)


def kernel(r_inputs, L0_rec_W0, L0_rec_b0, L0_rec_W1, L0_rec_b1, L0_rec_W2, L0_rec_b2, L0_rec_W_lin):
    import numpy as np
    import concourse.bacc as bacc
    from concourse.bass_utils import run_bass_kernel_spmd

    x, W0, W1, W2 = (np.asarray(a) for a in (r_inputs, L0_rec_W0, L0_rec_W1, L0_rec_W2))
    BATCH, M, K = x.shape
    F = W0.shape[1]
    H = F // 2
    BB = 1024 // K

    D = (M + 1) // 2
    xb = x.reshape(BATCH // BB, BB, M, K).transpose(0, 2, 3, 1).reshape(BATCH // BB, M, K * BB)
    xb = np.concatenate([xb, xb[:, 0:D - 1]], axis=1)

    C0, IC = 6, M - 32
    c, p = np.meshgrid(np.arange(C0), np.arange(128), indexing="ij")
    extra = (p >= 3 * M) & (c < 2) & (p < 3 * M + IC)
    d, i = np.where(extra, D - 2 + c, 3 * c + np.minimum(p // M, 2)), p % M
    split = np.arange(128) % 64
    d = np.concatenate([d, D - 2 + split[None] % 2]).T
    i = np.concatenate([i, IC + split[None] // 2]).T
    W0 = W0.reshape(M, M, F)
    w0, w0_mirror = W0[i, (i + d) % M], W0[(i + d) % M, i]

    T = M // 4
    chunks = [(0, t) for t in range(T + 1)] + [(1, t) for t in range(T)] + [(0, T + 1)]
    q, r = np.divmod(np.arange(128), 32)
    h = np.stack([32 * ((q + a) % 2) + r for a, _ in chunks], axis=1)
    m = np.stack([4 * t + q if t < T else 4 * T + q // 2 if t == T else 0 * q + M - 1 for _, t in chunks], axis=1)
    w1, w2 = W1[h * M + m], W2[h * M + m][:, :, 0:H]

    ins = {"x": xb, "w0": w0, "w0_mirror": w0_mirror, "w1": w1, "w2": w2,
           "b0": np.asarray(L0_rec_b0).reshape(F, 1), "b1": np.asarray(L0_rec_b1).reshape(F, 1),
           "b2": np.asarray(L0_rec_b2).reshape(F, 1), "w_lin": np.asarray(L0_rec_W_lin)}
    nc = bacc.Bacc("TRN2", target_bir_lowering=False, num_devices=1, dynamic_dma_scratch_size=1024)
    arrays, args = {}, []
    for name, v in ins.items():
        arrays[name] = np.ascontiguousarray(v)
        args.append(nc.dram_tensor(name, v.shape, mybir.dt.from_np(v.dtype), kind="ExternalInput").ap())
    args.append(nc.dram_tensor("out", (4, BATCH // 4), F32, kind="ExternalOutput").ap())
    cin_kernel(nc, *args, (BATCH, M, K, F))
    r = run_bass_kernel_spmd(nc, [arrays], core_ids=[0])
    return r.results[0]["out"].reshape(BATCH, 1)
```

```python
from contextlib import ExitStack

import concourse.bass as bass
from concourse import mybir

F32 = mybir.dt.float32
ALU = mybir.AluOpType
ACT = mybir.ActivationFunctionType

P = 128
QUAD = 32
BANK = 512


def cin_kernel(nc, x, w0, w0_mirror, w1, w2, b0, b1, b2, w_lin, out, dims):
    BATCH, M, K, F = dims
    HALF = F // 2
    NBLK = x.shape[0]
    NB = x.shape[2]
    BB = NB // K
    D = (M + 1) // 2
    DPC = P // M
    C0 = (D - 2) // DPC
    IC = M - QUAD
    ROWS0 = [DPC * M + (IC if c < 2 else 0) for c in range(C0)]
    QPT = P // QUAD
    T = M // QPT
    T2, T1 = T, T + 1
    CHUNKS = [(0, t) for t in range(T)] + [(0, T2)] + [(1, t) for t in range(T)] + [(0, T1)]
    CH = len(CHUNKS)
    X0_GROUPS = [(0, 1), (1, 2), (2, 4), (4, C0)]
    XB_GROUPS = [(0, 1), (1, 3), (3, 5), (5, T)]
    NH = NB // BANK
    RING = 10
    U = 2
    assert NH == 2 and 2 * CH % RING == 0 and NBLK % U == 0 and HALF == 2 * QUAD and M == QPT * T + 3
    assert D == DPC * C0 + 2 and DPC * M + IC <= P
    STEPS = NBLK // U
    ROT_LOADS = [DPC + 1, DPC + 1, DPC, DPC]
    BC_LOADS = [QPT] * len(XB_GROUPS) + [3]
    SMALL = 7
    assert BATCH == P // QUAD * BANK

    with ExitStack() as ctx:
        def sb(name, shape):
            return ctx.enter_context(nc.sbuf_tensor(name, shape, F32))

        def ps(name, shape):
            return ctx.enter_context(nc.psum_tensor(name, shape, F32))

        def sem(name):
            return ctx.enter_context(nc.semaphore(name))

        w0_sb = sb("w0_sb", [P, C0 + 1, F])
        w1_sb = sb("w1_sb", [P, CH, F])
        w2_sb = sb("w2_sb", [P, CH, HALF])
        bias = sb("bias", [P, 3])
        wl_col = sb("wl_col", [P, 2])
        ones = sb("ones", [P, QUAD])
        x_rep = sb("x_rep", [P, NB])
        x_rot = sb("x_rot", [P, C0, NB])
        x_rep_s = sb("x_rep_s", [P, BANK])
        x_rot_s = sb("x_rot_s", [P, BANK])
        x_bc = sb("x_bc", [P, U, T + 2, NB])
        prev = [[sb(f"prev{l}{a}", [P, NB]) for a in range(2)] for l in (1, 2)]
        prod = sb("prod", [P, RING, NB])
        w0m_sb = prod[:, RING - 1, 0:(C0 + 1) * F].rearrange("p (c f) -> p c f", f=F)
        res01 = sb("res01", [P, NB])
        res2 = sb("res2", [P, BANK])
        sum01 = sb("sum01", [P, BB])
        sum2 = sb("sum2", [P, BB])
        pool01 = sb("pool01", [P, BATCH])
        pool2 = sb("pool2", [P, BB + BATCH])
        y_sb = sb("y_sb", [P, BANK])

        acc0 = ps("acc0", [P, NH, BANK])
        acc1 = ps("acc1", [P, NH, BANK])
        acc2 = ps("acc2", [P, BANK])
        acc_y = ps("acc_y", [P, BANK])

        w0_loaded = sem("w0_loaded")
        w0_cleared = sem("w0_cleared")
        w0_ready = sem("w0_ready")
        w1_loaded = sem("w1_loaded")
        w2_loaded = sem("w2_loaded")
        small_loaded = sem("small_loaded")
        ones_ready = sem("ones_ready")
        split_loaded = sem("split_loaded")
        rep_loaded = sem("rep_loaded")
        rot_loaded = [sem(f"rot_loaded{g}") for g in range(len(X0_GROUPS))]
        bc_loaded = [[sem(f"bc_loaded{u}{g}") for g in range(len(XB_GROUPS) + 1)]
                     for u in range(U)]
        prod0_ready = sem("prod0_ready")
        prod_ready = sem("prod_ready")
        chunk_used = sem("chunk_used")
        acc0_full = sem("acc0_full")
        prev_ready = [sem(f"prev{l}_ready") for l in (1, 2)]
        res01_ready = sem("res01_ready")
        res2_ready = sem("res2_ready")
        res2_cleared = sem("res2_cleared")
        sum01_ready = sem("sum01_ready")
        sum2_ready = sem("sum2_ready")
        pooled = sem("pooled")
        y_ready = sem("y_ready")
        y_copied = sem("y_copied")
        y_stored = sem("y_stored")

        block = ctx.enter_context(nc.Block())

        @block.sync
        def _(sp):
            def rows_of(i, first, ap, col=0):
                base = x[i, first:first + 1, col:NB]
                return bass.AP(tensor=base.tensor, offset=base.offset, ap=ap)

            def load_pairs(i):
                for h in range(NH):
                    rows = slice(HALF * h, HALF * h + HALF)
                    src = rows_of(i, IC, [[NB, QUAD], [0, 2], [1, BANK]], BANK * h)
                    sp.dma_start(x_rep_s[rows, :], src).then_inc(split_loaded, 16)
                    src = rows_of(i, IC + D - 2, [[NB, QUAD], [NB, 2], [1, BANK]], BANK * h)
                    sp.dma_start(x_rot_s[rows, :], src).then_inc(split_loaded, 16)
                for r, n in ((0, 48), (48, 48), (96, ROWS0[0] - 96)):
                    sp.dma_start(x_rep[r:r + n, :], x[i, r % M:r % M + n, :]).then_inc(rep_loaded, 16)
                for g, (c0, c1) in enumerate(X0_GROUPS):
                    for d in range(DPC):
                        src = rows_of(i, DPC * c0 + d, [[NB, M], [DPC * NB, c1 - c0], [1, NB]])
                        sp.dma_start(x_rot[M * d:M * d + M, c0:c1, :], src).then_inc(rot_loaded[g], 16)
                    if g < 2:
                        src = x[i, D - 2 + g:D - 2 + g + IC, :]
                        sp.dma_start(x_rot[DPC * M:DPC * M + IC, g, :], src).then_inc(rot_loaded[g], 16)

            def load_bc(i, u):
                for g, (t0, t1) in enumerate(XB_GROUPS):
                    for q in range(QPT):
                        src = rows_of(i, QPT * t0 + q, [[0, QUAD], [QPT * NB, t1 - t0], [1, NB]])
                        sp.dma_start(x_bc[QUAD * q:QUAD * q + QUAD, u, t0:t1, :], src).then_inc(bc_loaded[u][g], 16)
                for q in range(2):
                    src = rows_of(i, QPT * T + q, [[0, HALF], [1, NB]])
                    sp.dma_start(x_bc[HALF * q:HALF * q + HALF, u, T2, :], src).then_inc(bc_loaded[u][-1], 16)
                src = rows_of(i, M - 1, [[0, P], [1, NB]])
                sp.dma_start(x_bc[:, u, T1, :], src).then_inc(bc_loaded[u][-1], 16)

            load_pairs(0)
            sp.dma_start(bias[:, 0:1], b0).then_inc(small_loaded, 16)
            sp.dma_start(bias[:, 1:2], b1).then_inc(small_loaded, 16)
            for g in range(2):
                sp.dma_start(bias[HALF * g:HALF * g + HALF, 2:3], b2[0:HALF, :]).then_inc(small_loaded, 16)
                sp.dma_start(wl_col[HALF * g:HALF * g + HALF, 1:2],
                             w_lin[2 * HALF:3 * HALF, :]).then_inc(small_loaded, 16)
            sp.dma_start(wl_col[:, 0:1], w_lin[0:2 * HALF, :]).then_inc(small_loaded, 16)
            sp.dma_start(w1_sb[:], w1).then_inc(w1_loaded, 16)
            load_bc(0, 0)
            sp.dma_start(w2_sb[:], w2).then_inc(w2_loaded, 16)
            sp.wait_ge(acc0_full, 1)
            load_pairs(1)
            load_bc(1, 1)
            with sp.Fori(0, STEPS - 1) as j:
                for u in range(U):
                    i = j * U + u
                    sp.wait_ge(acc0_full, i + 2)
                    load_pairs(i + 2)
                    sp.wait_ge(prod_ready, i * (2 * CH) + 2 * CH)
                    load_bc(i + 2, u)

            sp.wait_ge(y_copied, 1)
            y_rows = y_sb[0:P - QUAD + 1:QUAD, :]
            sp.dma_start(out, y_rows).then_inc(y_stored, 16)
            sp.wait_ge(y_stored, 16)

        @block.vector
        def _(dve):
            def products0(i):
                dve.wait_ge(split_loaded, i * (32 * NH) + 32 * NH)
                nc.vector.tensor_tensor(x_rot_s[:], x_rot_s[:], x_rep_s[:], ALU.mult).then_inc(prod0_ready, 1)
                dve.wait_ge(rep_loaded, i * (16 * 3) + 16 * 3)
                for g, (c0, c1) in enumerate(X0_GROUPS):
                    dve.wait_ge(rot_loaded[g], i * (16 * ROT_LOADS[g]) + 16 * ROT_LOADS[g])
                    for c in range(c0, c1):
                        r = x_rot[0:ROWS0[c], c, :]
                        nc.vector.tensor_tensor(r, r, x_rep[0:ROWS0[c], :], ALU.mult).then_inc(prod0_ready, 1)

            def products(i, j, u, layer):
                first = i * (2 * CH) + (layer - 1) * CH
                group = {t0: g for g, (t0, _) in enumerate(XB_GROUPS)}
                group[T2] = len(XB_GROUPS)
                for c, (a, t) in enumerate(CHUNKS):
                    if layer == 1 and a == 0 and t in group:
                        n = 16 * BC_LOADS[group[t]]
                        dve.wait_ge(bc_loaded[u][group[t]], j * n + n)
                    if t == 0:
                        dve.wait_ge(prev_ready[layer - 1], i * 2 + a + 1)
                    dve.wait_ge(chunk_used, first + c + 1)
                    s = ((layer - 1) * CH + c) % RING
                    old, new = prev[layer - 1][a], x_bc[:, u, t, :]
                    if t < T1:
                        mul = nc.vector.tensor_tensor(prod[:, s, :], old[:], new, ALU.mult)
                    elif layer == 2:
                        mul = nc.vector.tensor_tensor(prod[0:HALF, s, :], old[0:HALF, :], new[0:HALF], ALU.mult)
                    else:
                        for h in range(NH):
                            k, n = slice(HALF * h, HALF * h + HALF), slice(BANK * h, BANK * h + BANK)
                            mul = nc.vector.tensor_tensor(prod[k, s, n], old[k, n], new[k, n], ALU.mult)
                    mul.then_inc(prod_ready, 1)
                    if layer == 2 and c == RING:
                        dve.wait_ge(res01_ready, i * 2 + 3)
                        channel_sum(sum01, res01).then_inc(sum01_ready, 1)

            def channel_sum(total, res):
                return nc.vector.tensor_reduce(total[:], res[:].rearrange("p (k b) -> p b k", b=BB),
                                               mybir.AxisListType.X, ALU.add)

            def channel_sum2(i):
                dve.wait_ge(res2_ready, i + 1)
                channel_sum(sum2, res2).then_inc(sum2_ready, 1)

            nc.vector.memset(ones[:], 1.0).then_inc(ones_ready, 1)
            nc.vector.memset(res2[:], 0.0).then_inc(res2_cleared, 1)
            dve.sem_inc(sum01_ready, 1)
            dve.wait_ge(w0_loaded, 32)
            nc.vector.memset(w0m_sb[0:M, 0, :], 0.0).then_inc(w0_cleared, 1)
            dve.wait_ge(w0_cleared, 1)
            nc.vector.tensor_tensor(w0_sb[:], w0_sb[:], w0m_sb, ALU.add).then_inc(w0_ready, 1)
            products0(0)
            with dve.Fori(0, STEPS - 1) as j:
                for u in range(U):
                    i = j * U + u
                    products(i, j, u, 1)
                    channel_sum2(i)
                    products0(i + 1)
                    products(i, j, u, 2)
            for u in range(U):
                i = (STEPS - 1) * U + u
                products(i, STEPS - 1, u, 1)
                channel_sum2(i)
                if u < U - 1:
                    products0(i + 1)
                products(i, STEPS - 1, u, 2)
            channel_sum2(NBLK)

            dve.wait_ge(y_ready, 1)
            nc.vector.tensor_copy(y_sb[:], acc_y[:]).then_inc(y_copied, 1)

        @block.tensor
        def _(pe):
            def split(acc, w, rhs, start, stop):
                for h in range(NH):
                    k = slice(HALF * h, HALF * h + HALF)
                    mm = nc.tensor.matmul(acc[:, h, :], w[k, :], rhs[h], start=start, stop=stop)
                return mm

            def full(acc, w, rhs, start, stop):
                for h in range(NH):
                    mm = nc.tensor.matmul(acc[:, h, :], w, rhs[:, BANK * h:BANK * h + BANK], start=start, stop=stop)
                return mm

            def keep_warm(n):
                for _ in range(n):
                    nc.tensor.matmul(acc_y[:], res2[:, 0:P], res2[:], start=True, stop=True)

            def layer0(i, first=False):
                if not first:
                    pe.wait_ge(res01_ready, i * 2)
                pe.wait_ge(prod0_ready, i * (C0 + 1) + 1)
                split(acc0, w0_sb[:, C0, :], [x_rot_s[0:HALF, :], x_rot_s[HALF:P, :]], True, False)
                for c in range(C0):
                    pe.wait_ge(prod0_ready, i * (C0 + 1) + c + 2)
                    k = ROWS0[c]
                    mm = full(acc0, w0_sb[0:k, c, :], x_rot[0:k, c, :], False, c == C0 - 1)
                mm.then_inc(acc0_full, 1)

            def layer1(i):
                pe.wait_ge(res01_ready, i * 2 + 1)
                for c in range(CH):
                    pe.wait_ge(prod_ready, i * (2 * CH) + c + 1)
                    s = c % RING
                    if c < CH - 1:
                        mm = full(acc1, w1_sb[:, c, :], prod[:, s, :], c == 0, False)
                    else:
                        mm = split(acc1, w1_sb[:, c, :], [prod[0:HALF, s, 0:BANK], prod[HALF:P, s, BANK:NB]],
                                   False, True)
                    mm.then_inc(chunk_used, 1)

            def layer2(i):
                pe.wait_ge(w2_loaded, 16)
                pe.wait_ge(res2_ready, i + 1)
                for c in range(CH):
                    if c < CH - 1:
                        pe.wait_ge(prod_ready, i * (2 * CH) + CH + (c + 1 if c < CH - 2 else CH))
                    k = P if c < CH - 1 else HALF
                    for h in range(NH):
                        mm = nc.tensor.matmul(acc2[HALF * h:HALF * h + HALF, :], w2_sb[0:k, c, :],
                                              prod[0:k, (CH + c) % RING, BANK * h:BANK * h + BANK],
                                              start=(c == 0), stop=(c == CH - 1))
                    mm.then_inc(chunk_used, 1)

            pe.sem_inc(chunk_used, RING)
            pe.wait_ge(res2_cleared, 1)
            keep_warm(5)
            pe.wait_ge(w0_ready, 1)
            layer0(0, first=True)
            keep_warm(4)
            pe.wait_ge(w1_loaded, 16)
            with pe.Fori(0, STEPS - 1) as j:
                for u in range(U):
                    i = j * U + u
                    layer1(i)
                    layer0(i + 1)
                    layer2(i)
            for u in range(U):
                i = (STEPS - 1) * U + u
                layer1(i)
                if u < U - 1:
                    layer0(i + 1)
                layer2(i)

            pe.wait_ge(ones_ready, 1)
            for g, (pool, skip) in enumerate(((pool01, 0), (pool2, BB))):
                pe.wait_ge(pooled, 2 * NBLK + g)
                for q in range(P // QUAD):
                    mm = nc.tensor.matmul(acc_y[QUAD * q:QUAD * q + QUAD, :], ones[:],
                                          pool[:, skip + BANK * q:skip + BANK * q + BANK],
                                          start=(g == 0), stop=(g == 1))
            mm.then_inc(y_ready, 1)

        @block.scalar
        def _(act):
            def spread(dst, acc, layer):
                src = acc[HALF:P, :, :].rearrange("p h n -> p (h n)")
                for g in range(2):
                    op = nc.scalar.activation(dst[0][HALF * g:HALF * g + HALF, :], src, ACT.Relu,
                                              bias=bias[HALF:P, layer:layer + 1])
                op.then_inc(prev_ready[layer], 1)
                for q in range(QPT):
                    h = HALF + QUAD * ((q + 1) % 2)
                    op = nc.scalar.activation(dst[1][QUAD * q:QUAD * q + QUAD, :],
                                              acc[h:h + QUAD, :, :].rearrange("p h n -> p (h n)"), ACT.Relu,
                                              bias=bias[h:h + QUAD, layer:layer + 1])
                op.then_inc(prev_ready[layer], 1)

            def keep01(acc, layer):
                nc.scalar.activation(res01[HALF * layer:HALF * layer + HALF, :],
                                     acc[0:HALF, :, :].rearrange("p h n -> p (h n)"), ACT.Relu,
                                     bias=bias[0:HALF, layer:layer + 1]).then_inc(res01_ready, 1)

            def evacuate0(i):
                act.wait_ge(acc0_full, i + 1)
                spread(prev[0], acc0, 0)
                act.wait_ge(sum01_ready, i + 1)
                keep01(acc0, 0)

            def evacuate1(i):
                act.wait_ge(chunk_used, i * (2 * CH) + RING + CH)
                spread(prev[1], acc1, 1)
                keep01(acc1, 1)

            def evacuate2(i):
                act.wait_ge(chunk_used, i * (2 * CH) + RING + 2 * CH)
                act.wait_ge(sum2_ready, i + 1)
                nc.scalar.activation(res2[:], acc2[:], ACT.Relu, bias=bias[:, 2:3]).then_inc(res2_ready, 1)

            def weigh(pool, column, total, g):
                act.wait_ge(small_loaded, 16 * SMALL)
                nc.scalar.activation(pool[:, bass.ds(column, BB)], total[:], ACT.Copy,
                                     scale=wl_col[:, g:g + 1]).then_inc(pooled, 1)

            def weigh01(i):
                act.wait_ge(sum01_ready, i + 2)
                weigh(pool01, i * BB, sum01, 0)

            def weigh2(i):
                act.wait_ge(sum2_ready, i + 1)
                weigh(pool2, i * BB, sum2, 1)

            act.dma_start(w0_sb[:], w0).then_inc(w0_loaded, 16)
            act.dma_start(w0m_sb, w0_mirror).then_inc(w0_loaded, 16)
            act.sem_inc(res01_ready, 1)
            act.wait_ge(res2_cleared, 1)
            nc.scalar.activation(sum2[0:1, 0:1], res2[0:1, 0:1], ACT.Relu)
            act.sem_inc(res2_ready, 1)
            act.wait_ge(small_loaded, 16 * SMALL)
            evacuate0(0)
            with act.Fori(0, STEPS - 1) as j:
                for u in range(U):
                    i = j * U + u
                    weigh2(i)
                    evacuate1(i)
                    evacuate0(i + 1)
                    weigh01(i)
                    evacuate2(i)
            for u in range(U):
                i = (STEPS - 1) * U + u
                weigh2(i)
                evacuate1(i)
                if u < U - 1:
                    evacuate0(i + 1)
                weigh01(i)
                evacuate2(i)
            weigh2(NBLK)


def kernel(r_inputs, L0_rec_W0, L0_rec_b0, L0_rec_W1, L0_rec_b1, L0_rec_W2, L0_rec_b2, L0_rec_W_lin):
    import numpy as np
    import concourse.bacc as bacc
    from concourse.bass_utils import run_bass_kernel_spmd

    x, W0, W1, W2 = (np.asarray(a) for a in (r_inputs, L0_rec_W0, L0_rec_W1, L0_rec_W2))
    BATCH, M, K = x.shape
    F = W0.shape[1]
    H = F // 2
    BB = 1024 // K

    D = (M + 1) // 2
    xb = x.reshape(BATCH // BB, BB, M, K).transpose(0, 2, 3, 1).reshape(BATCH // BB, M, K * BB)
    xb = np.concatenate([xb, xb[:, 0:D - 1]], axis=1)

    C0, IC = 6, M - 32
    c, p = np.meshgrid(np.arange(C0), np.arange(128), indexing="ij")
    extra = (p >= 3 * M) & (c < 2) & (p < 3 * M + IC)
    d, i = np.where(extra, D - 2 + c, 3 * c + np.minimum(p // M, 2)), p % M
    split = np.arange(128) % 64
    d = np.concatenate([d, D - 2 + split[None] % 2]).T
    i = np.concatenate([i, IC + split[None] // 2]).T
    W0 = W0.reshape(M, M, F)
    w0, w0_mirror = W0[i, (i + d) % M], W0[(i + d) % M, i]

    T = M // 4
    chunks = [(0, t) for t in range(T + 1)] + [(1, t) for t in range(T)] + [(0, T + 1)]
    q, r = np.divmod(np.arange(128), 32)
    h = np.stack([32 * ((q + a) % 2) + r for a, _ in chunks], axis=1)
    m = np.stack([4 * t + q if t < T else 4 * T + q // 2 if t == T else 0 * q + M - 1 for _, t in chunks], axis=1)
    w1, w2 = W1[h * M + m], W2[h * M + m][:, :, 0:H]

    ins = {"x": xb, "w0": w0, "w0_mirror": w0_mirror, "w1": w1, "w2": w2,
           "b0": np.asarray(L0_rec_b0).reshape(F, 1), "b1": np.asarray(L0_rec_b1).reshape(F, 1),
           "b2": np.asarray(L0_rec_b2).reshape(F, 1), "w_lin": np.asarray(L0_rec_W_lin)}
    nc = bacc.Bacc("TRN2", target_bir_lowering=False, num_devices=1, dynamic_dma_scratch_size=1024)
    arrays, args = {}, []
    for name, v in ins.items():
        arrays[name] = np.ascontiguousarray(v)
        args.append(nc.dram_tensor(name, v.shape, mybir.dt.from_np(v.dtype), kind="ExternalInput").ap())
    args.append(nc.dram_tensor("out", (4, BATCH // 4), F32, kind="ExternalOutput").ap())
    cin_kernel(nc, *args, (BATCH, M, K, F))
    r = run_bass_kernel_spmd(nc, [arrays], core_ids=[0])
    return r.results[0]["out"].reshape(BATCH, 1)
```
